# Optimizing a Trainium2 kernel written in Bass

```python
import numpy as np
import jax
import jax.numpy as jnp

def _softmax(x, axis=-1):
    return jax.nn.softmax(x, axis=axis)
def _gelu(x):
    return jax.nn.gelu(x, approximate=True)
def _silu(x):
    return jax.nn.silu(x)
def _sigmoid(x):
    return jax.nn.sigmoid(x)
def _layernorm(x, axis=-1, eps=1e-5):
    m = jnp.mean(x, axis=axis, keepdims=True)
    v = jnp.var(x, axis=axis, keepdims=True)
    return (x - m) / jnp.sqrt(v + eps)
def _scatter_add(tgt, idx, src, axis=0):
    return tgt.at[idx].add(src)
def _segment_sum(src, seg, n):
    return jax.ops.segment_sum(src, seg, n)

kernel_name = 'mk_conv_seq_d1_conv_nchw256_a87c47'

def setup_inputs(seed: int = 0):
    np.random.seed(seed)
    _w = jnp.asarray
    def _rec_inputs():
        import jax
        import jax.numpy as jnp
        _gk = jax.random.key(seed)
        x = -0.000125 + 0.9999 * jax.random.normal(jax.random.fold_in(_gk, 1), (32, 256, 64, 64), jnp.float32)
        return x
    x = _rec_inputs()
    def _L0_conv_setup():
        import jax, jax.numpy as jnp
        import numpy as np
        H_SIZE = 64

        def _hadamard(n):
            H = np.array([[1.0]], dtype=np.float32)
            while H.shape[0] < n:
                H = np.block([[H, H], [H, -H]])
            return jnp.asarray(H)
        key = jax.random.key(seed)
        k1, k2, k3, k4 = jax.random.split(key, 4)
        B, C_in, C_out, P = (32, 256, 256, 2)
        x = jax.random.normal(k1, (B, C_in, H_SIZE, H_SIZE), dtype=jnp.float32)
        v = jax.random.uniform(k2, (P, H_SIZE, H_SIZE), dtype=jnp.float32)
        W = jax.random.normal(k3, (P, C_out, C_in), dtype=jnp.float32) * (1.0 / np.sqrt(C_in))
        T = jax.random.uniform(k4, (P, H_SIZE, H_SIZE), dtype=jnp.float32) * 0.1
        return {'x': x, 'v': v, 'W': W, 'T': T}
    _L0_conv_all = _L0_conv_setup()
    _L0_conv_in = {k: v for k, v in _L0_conv_all.items() if k in ('v', 'W', 'T', )}
    del _L0_conv_all

    return {
        "x": x,
        "L0_conv_v": _L0_conv_in["v"],
        "L0_conv_W": _L0_conv_in["W"],
        "L0_conv_T": _L0_conv_in["T"],
    }

def reference(x, L0_conv_v, L0_conv_W, L0_conv_T):
    import jax
    import jax.numpy as jnp
    def _L0_conv_ref(x, v, W, T):
        import jax, jax.numpy as jnp
        import numpy as np
        H_SIZE = 64

        def _hadamard(n):
            H = np.array([[1.0]], dtype=np.float32)
            while H.shape[0] < n:
                H = np.block([[H, H], [H, -H]])
            return jnp.asarray(H)
        n = H_SIZE
        H = _hadamard(n)
        f1 = jnp.einsum('bchw,wk->bchk', x, H)
        f2 = jnp.einsum('bchw,hk->bckw', f1, H)
        f3 = v[:, None, None, :, :] * f2[None]
        f4 = jnp.einsum('poc,pbchw->pbohw', W, f3)
        f5 = jnp.sign(f4) * jnp.maximum(jnp.abs(f4) - T[:, None, None, :, :], 0.0)
        f6 = f5.sum(axis=0)
        f7 = jnp.einsum('bchw,wk->bchk', f6, H) / n
        f8 = jnp.einsum('bchw,hk->bckw', f7, H) / n
        return f8 + x

    def _gn(v, G=32, eps=1e-5):
        B_, C_, H_, W_ = v.shape
        g = v.reshape(B_, G, C_ // G, H_, W_)
        m = jnp.mean(g, axis=(2, 3, 4), keepdims=True)
        s = jnp.var(g, axis=(2, 3, 4), keepdims=True)
        return ((g - m) / jnp.sqrt(s + eps)).reshape(v.shape)

    def _ln_c(v, eps=1e-6):
        m = jnp.mean(v, axis=1, keepdims=True)
        s = jnp.var(v, axis=1, keepdims=True)
        return (v - m) / jnp.sqrt(s + eps)

    def _ln_t(v, eps=1e-5):
        m = jnp.mean(v, axis=-1, keepdims=True)
        s = jnp.var(v, axis=-1, keepdims=True)
        return (v - m) / jnp.sqrt(s + eps)

    def _to_tokens(v):
        B_, C_, H_, W_ = v.shape
        return v.reshape(B_, C_, H_ * W_).transpose(0, 2, 1)
    def _from_tokens(t, like):
        B_, C_, H_, W_ = like.shape
        return t.transpose(0, 2, 1).reshape(B_, C_, H_, W_)

    x = _L0_conv_ref(x, L0_conv_v, L0_conv_W, L0_conv_T)
    return x


_drawn_inputs = setup_inputs


def setup_inputs(seed=0):
    import zlib

    import numpy as np

    out = dict(_drawn_inputs(seed))
    spreads = {}
    factors = {'L0_conv_T': 64.0}
    for name, (base, spread) in spreads.items():
        noise = np.random.default_rng([zlib.crc32(name.encode()), seed]).standard_normal(out[name].shape)
        drawn = base * np.exp(spread * noise) if base else spread * noise
        out[name] = jnp.asarray(drawn.astype(out[name].dtype))
    for name, factor in factors.items():
        out[name] = (out[name] * factor).astype(out[name].dtype)
    return out
```

```python
import concourse.bass as bass
from concourse import mybir
from contextlib import ExitStack


def spectral_conv_kernel(nc, x, v, W, T, h_outer, h_inner, eye, out):
    f32 = mybir.dt.float32
    f32r = mybir.dt.float32r
    ALU = mybir.AluOpType
    ACT = mybir.ActivationFunctionType

    B, C, HH, WW = x.shape
    P = W.shape[0]
    L = 128
    N = HH * WW
    R = N // L
    CA = L // R
    CB = C // CA
    HALF = C // L
    BANK = 512
    TPB = BANK // L
    G1 = CB // TPB
    RPG = BANK // (HALF * L)
    G2 = R // RPG
    NCH = 8
    GPC = G1 // NCH
    PO = P * C
    FR = 4
    PAIRS = B // 2
    assert PO == BANK and C == HALF * L and CB % NCH == 0

    x_v = x.rearrange("b (cb ca) (a h) w -> b (ca a) cb (h w)", ca=CA, a=R)
    out_v = out.rearrange("b (cb ca) (a h) w -> b (ca a) cb (h w)", ca=CA, a=R)
    w_v = W.rearrange("p (oh q) c -> q p oh c", q=L)
    v_v = v.rearrange("p (r h) w -> (p r) (h w)", r=R)
    t_v = T.rearrange("p (r h) w -> (p r) (h w)", r=R)

    ctx = ExitStack()
    with ctx:
        def sb(name, shape, dt):
            return ctx.enter_context(nc.sbuf_tensor(name, shape, dt))

        def sem(name):
            return ctx.enter_context(nc.semaphore(name))

        xs = sb("xs", [L, 2, CB, L], f32)
        f1 = sb("f1", [L, R, CB, CA], f32)
        f2hi = sb("f2hi", [L, 2, RPG, HALF, L], f32r)
        f2lo = sb("f2lo", [L, 2, RPG, HALF, L], f32r)
        f4 = sb("f4", [L, FR, RPG, P, C], f32)
        clipped = sb("clipped", [L, RPG, P, C], f32)
        excess = sb("excess", [L, RPG, P, C], f32)
        f6 = sb("f6", [L, C, R], f32)
        f7hi = sb("f7hi", [L, 2, BANK], f32r)
        f7lo = sb("f7lo", [L, 2, BANK], f32r)
        w_nat = sb("w_nat", [L, P, HALF, C], f32)
        wThi = sb("wThi", [L, HALF, PO], f32r)
        wTlo = sb("wTlo", [L, HALF, PO], f32r)
        vt_nat = sb("vt_nat", [L, L], f32)
        vt = sb("vt", [L, 2, P, R], f32)
        neg_t = sb("neg_t", [L, P, R], f32)
        h32 = sb("h32", [L, L], f32)
        h32r = sb("h32r", [L, L], f32r)
        h128 = sb("h128", [L, L], f32)
        ident = sb("ident", [L, L], f32)
        ps = ctx.enter_context(nc.psum_tensor("ps", [L, 8, BANK], f32))
        S2, S3 = 2, 4

        consts_in = sem("consts_in")
        w_in = sem("w_in")
        vt_in = sem("vt_in")
        x_in = [sem(f"x_in{k}") for k in range(NCH)]
        y_out = [sem(f"y_out{k}") for k in range(NCH)]
        w_turned = sem("w_turned")
        vt_turned = sem("vt_turned")
        wT_hi = sem("wT_hi")
        wT_ready = sem("wT_ready")
        vt_ready = sem("vt_ready")
        negt_ready = sem("negt_ready")
        h32r_ready = sem("h32r_ready")
        step1_done = sem("step1_done")
        f1_ready = sem("f1_ready")
        step2_done = sem("step2_done")
        f2hi_ready = sem("f2hi_ready")
        f2lo_ready = sem("f2lo_ready")
        step3_done = sem("step3_done")
        f4_ready = sem("f4_ready")
        clip_ready = sem("clip_ready")
        excess_ready = sem("excess_ready")
        f6_ready = sem("f6_ready")
        step4_done = sem("step4_done")
        f7hi_ready = sem("f7hi_ready")
        f7lo_ready = sem("f7lo_ready")
        step5_done = sem("step5_done")
        y_ready = sem("y_ready")
        F6_0 = FR
        Y_0 = 4

        block = ctx.enter_context(nc.Block())

        def images(eng, image):
            with eng.Fori(0, PAIRS - 1) as it:
                for s in range(2):
                    image(it * 2 + s, s, False, False)
            for s in range(2):
                image(B - 2 + s, s, True, s == 1)

        @block.sync
        def _(sp):
            sp.dma_start(h32[:], h_outer).then_inc(consts_in, 16)
            for k in range(NCH):
                q = slice(k * CB // NCH, (k + 1) * CB // NCH)
                sp.dma_start(xs[:, 0, q, :], x_v[0, :, q, :]).then_inc(x_in[k], 16)
            sp.dma_start(ident[:], eye).then_inc(consts_in, 16)
            sp.dma_start(h128[:], h_inner).then_inc(consts_in, 16)
            sp.dma_start(vt_nat[0:P * R, :], v_v).then_inc(vt_in, 16)
            sp.dma_start(vt_nat[P * R:2 * P * R, :], t_v).then_inc(vt_in, 16)
            for p in range(P):
                sp.dma_start(w_nat[:, p, :, :], w_v[:, p, :, :]).then_inc(w_in, 16)
            for k in range(NCH):
                q = slice(k * CB // NCH, (k + 1) * CB // NCH)
                sp.wait_ge(x_in[k], 16)
                sp.dma_start(xs[:, 1, q, :], x_v[1, :, q, :]).then_inc(x_in[k], 16)

            def image(b, slot, last_pair, last):
                for k in range(NCH):
                    q = slice(k * CB // NCH, (k + 1) * CB // NCH)
                    sp.wait_ge(y_ready, Y_0 + G1 * b + GPC * (k + 1))
                    if last_pair:
                        sp.dma_start(out_v[b, :, q, :], xs[:, slot, q, :]).then_inc(y_out[k], 16)
                    else:
                        sp.dma_start(out_v[bass.ds(b, 1), :, q, :].rearrange("b p c j -> p (b c) j"),
                                     xs[:, slot, q, :]).then_inc(y_out[k], 16)
                if not last_pair:
                    for k in range(NCH):
                        q = slice(k * CB // NCH, (k + 1) * CB // NCH)
                        sp.wait_ge(y_out[k], 16 * (b + 1))
                        sp.dma_start(xs[:, slot, q, :],
                                     x_v[bass.ds(b + 2, 1), :, q, :].rearrange("b p c j -> p (b c) j")
                                     ).then_inc(x_in[k], 16)

            images(sp, image)
            for k in range(NCH):
                sp.wait_ge(y_out[k], 16 * B)

        @block.tensor
        def _(pe):
            def step1(b, slot):
                for g in range(G1):
                    if g % GPC == 0:
                        pe.wait_ge(x_in[g // GPC], 16 * (b + 1))
                    if g >= 4:
                        pe.wait_ge(f1_ready, G1 * b + g - 3)
                    for t in range(TPB):
                        mm = nc.tensor.matmul(ps[:, g % 4, t * L:(t + 1) * L], xs[:, slot, g * TPB + t, :],
                                              h32[:], start=True, stop=True)
                    mm.then_inc(step1_done, 1)

            def step2(b, g):
                if g == 0:
                    pe.wait_ge(f1_ready, G1 * (b + 1))
                for t in range(TPB):
                    r, half = g * RPG + t // HALF, t % HALF
                    mm = nc.tensor.matmul(ps[:, S2 + g % 2, t * L:(t + 1) * L],
                                          f1[:, r, half * CB // 2:(half + 1) * CB // 2, :].rearrange("p b a -> p (b a)"),
                                          h128[:], start=True, stop=True)
                mm.then_inc(step2_done, 1)

            def step3(b, g):
                s = g % 2
                for k in range(RPG):
                    r = g * RPG + k
                    bank = ps[:, S3 + r % 4, :]
                    if r < 4:
                        pe.wait_ge(y_ready, Y_0 + G1 * b + r - 3)
                    else:
                        pe.wait_ge(f4_ready, R * b + r - 3)
                    if k == 0:
                        pe.wait_ge(f2hi_ready, G2 * b + g + 1)
                    for half in range(HALF):
                        nc.tensor.matmul(bank, f2hi[:, s, k, half, :], wTlo[:, half, :], start=(half == 0), stop=False)
                        nc.tensor.matmul(bank, f2hi[:, s, k, half, :], wThi[:, half, :], start=False, stop=False)
                    if k == 0:
                        pe.wait_ge(f2lo_ready, G2 * b + g + 1)
                    for half in range(HALF):
                        mm = nc.tensor.matmul(bank, f2lo[:, s, k, half, :], wThi[:, half, :],
                                              start=False, stop=(half == HALF - 1))
                    mm.then_inc(step3_done, 1)

            def step4(b, g):
                for t in range(TPB):
                    o = (g * TPB + t) * CA
                    mm = nc.tensor.matmul(ps[:, g % 2, t * L:(t + 1) * L],
                                          f6[:, o:o + CA, :].rearrange("p o r -> p (o r)"), h128[:],
                                          start=True, stop=True)
                mm.then_inc(step4_done, 1)

            def step5(b, g):
                bank = ps[:, S3 + g % 4, :]
                if g < 4:
                    pe.wait_ge(f4_ready, R * b + R - 3 + g)
                else:
                    pe.wait_ge(y_ready, Y_0 + G1 * b + g - 3)
                pe.wait_ge(f7hi_ready, G1 * b + g + 1)
                nc.tensor.matmul(bank, h32r[:], f7hi[:, g % 2, :], start=True, stop=False)
                pe.wait_ge(f7lo_ready, G1 * b + g + 1)
                nc.tensor.matmul(bank, h32r[:], f7lo[:, g % 2, :], start=False, stop=True).then_inc(step5_done, 1)

            pe.wait_ge(consts_in, 48)
            step1(0, 0)
            pe.wait_ge(w_in, 16 * P)
            for half in range(HALF):
                for po in range(P * HALF):
                    mm = nc.tensor.transpose(ps[:, S3 + half, po * L:(po + 1) * L],
                                             w_nat[:, po // HALF, po % HALF, half * L:(half + 1) * L], ident[:])
            mm.then_inc(w_turned, 1)
            pe.wait_ge(vt_in, 32)
            nc.tensor.transpose(ps[:, S3 + 2, 0:L], vt_nat[:], ident[:]).then_inc(vt_turned, 1)
            step2(0, 0)
            pe.wait_ge(wT_ready, 1)
            pe.wait_ge(vt_ready, 1)
            pe.wait_ge(h32r_ready, 1)

            def image(b, slot, last_pair, last):
                for g in range(G2):
                    if g + 1 < G2:
                        step2(b, g + 1)
                    step3(b, g)
                if not last:
                    step1(b + 1, 1 - slot)
                    pe.wait_ge(f1_ready, G1 * (b + 1) + G1 - 2)
                pe.wait_ge(f6_ready, F6_0 + G2 * (b + 1))
                step4(b, 0)
                for g in range(G1):
                    if g + 1 < G1:
                        step4(b, g + 1)
                    elif not last:
                        step2(b + 1, 0)
                    step5(b, g)

            images(pe, image)

        @block.scalar
        def _(act):
            def f1_from_step1(b):
                for g in range(G1):
                    act.wait_ge(step1_done, G1 * b + g + 1)
                    nc.scalar.copy(f1[:, :, g * TPB:(g + 1) * TPB, :].rearrange("j r cb ca -> j (cb ca) r"),
                                   ps[:, g % 4, :].rearrange("j (q r) -> j q r", r=R)).then_inc(f1_ready, 1)

            def f2_hi(b, g):
                act.wait_ge(step2_done, G2 * b + g + 1)
                if g >= 2:
                    act.wait_ge(step3_done, R * b + RPG * (g - 1))
                nc.scalar.copy(f2hi[:, g % 2, :, :, :].rearrange("c k h i -> c (k h i)"),
                               ps[:, S2 + g % 2, :]).then_inc(f2hi_ready, 1)

            def f4_from_step3(b, g):
                act.wait_ge(f6_ready, F6_0 + G2 * b + g + 1 - FR)
                for k in range(RPG):
                    r = g * RPG + k
                    act.wait_ge(step3_done, R * b + r + 1)
                    for p in range(P):
                        cp = nc.scalar.activation(f4[:, g % FR, k, p, :], ps[:, S3 + r % 4, p * C:(p + 1) * C],
                                                  ACT.Copy, scale=vt[:, 0, p, r:r + 1])
                    cp.then_inc(f4_ready, 1)

            act.wait_ge(consts_in, 48)
            nc.scalar.copy(h32r[:], h32[:]).then_inc(h32r_ready, 1)
            f1_from_step1(0)
            act.wait_ge(w_turned, 1)
            nc.scalar.copy(wThi[:], ps[:, S3:S3 + HALF, :]).then_inc(wT_hi, 1)
            act.wait_ge(vt_turned, 1)
            nc.scalar.copy(vt[:].rearrange("i t p r -> i (t p r)"), ps[:, S3 + 2, 0:L]).then_inc(vt_ready, 1)
            f2_hi(0, 0)
            act.wait_ge(vt_ready, 1)

            def image(b, slot, last_pair, last):
                for g in range(G2):
                    if g + 1 < G2:
                        f2_hi(b, g + 1)
                    f4_from_step3(b, g)
                if not last:
                    f1_from_step1(b + 1)
                for g in range(G1):
                    act.wait_ge(step4_done, G1 * b + g + 1)
                    if g >= 2:
                        act.wait_ge(step5_done, G1 * b + g - 1)
                    nc.scalar.copy(f7hi[:, g % 2, :], ps[:, g % 2, :]).then_inc(f7hi_ready, 1)
                if not last:
                    f2_hi(b + 1, 0)

            images(act, image)

        @block.vector
        def _(dve):
            def f2_lo(b, g):
                dve.wait_ge(f2hi_ready, G2 * b + g + 1)
                nc.vector.tensor_tensor(f2lo[:, g % 2, :, :, :].rearrange("c k h i -> c (k h i)"), ps[:, S2 + g % 2, :],
                                        f2hi[:, g % 2, :, :, :].rearrange("c k h i -> c (k h i)").bitcast(f32),
                                        ALU.subtract).then_inc(f2lo_ready, 1)

            def threshold(b, g):
                dve.wait_ge(f4_ready, R * b + RPG * (g + 1))
                for k in range(RPG):
                    r = g * RPG + k
                    for p in range(P):
                        cl = nc.vector.tensor_scalar(clipped[:, k, p, :], f4[:, g % FR, k, p, :],
                                                     vt[:, 1, p, r:r + 1], neg_t[:, p, r:r + 1], ALU.min, ALU.max)
                cl.then_inc(clip_ready, 1)
                dve.wait_ge(clip_ready, G2 * b + g + 1)
                nc.vector.tensor_tensor(excess[:], f4[:, g % FR, :, :, :], clipped[:],
                                        ALU.subtract).then_inc(excess_ready, 1)
                dve.wait_ge(excess_ready, G2 * b + g + 1)
                nc.vector.tensor_tensor(f6[:, :, g * RPG:(g + 1) * RPG].rearrange("i o k -> i k o"),
                                        excess[:, :, 0, :], excess[:, :, 1, :], ALU.add).then_inc(f6_ready, 1)

            def f7_lo(b, g):
                dve.wait_ge(f7hi_ready, G1 * b + g + 1)
                nc.vector.tensor_tensor(f7lo[:, g % 2, :], ps[:, g % 2, :], f7hi[:, g % 2, :].bitcast(f32),
                                        ALU.subtract).then_inc(f7lo_ready, 1)

            def residual(b, slot, g):
                dve.wait_ge(step5_done, G1 * b + g + 1)
                place = xs[:, slot, g * TPB:(g + 1) * TPB, :].rearrange("p c j -> p (c j)")
                nc.vector.scalar_tensor_tensor(place, ps[:, S3 + g % 4, :], 1.0 / N, place,
                                               ALU.mult, ALU.add).then_inc(y_ready, 1)

            dve.wait_ge(wT_hi, 1)
            nc.vector.tensor_tensor(wTlo[:], ps[:, S3:S3 + HALF, :], wThi[:].bitcast(f32),
                                    ALU.subtract).then_inc(wT_ready, 1)
            dve.wait_ge(vt_ready, 1)
            nc.vector.tensor_scalar(neg_t[:], vt[:, 1, :, :], -1.0, None, ALU.mult).then_inc(negt_ready, 1)
            f2_lo(0, 0)
            dve.wait_ge(negt_ready, 1)
            nc.vector.memset(clipped[:, 0, 0, 0:1], 0.0).then_inc(f6_ready, F6_0)
            nc.vector.memset(clipped[:, 0, 0, 1:2], 0.0).then_inc(y_ready, Y_0)
            dve.wait_ge(y_ready, Y_0)

            def image(b, slot, last_pair, last):
                for g in range(G2):
                    if g + 1 < G2:
                        f2_lo(b, g + 1)
                    if g >= 1:
                        threshold(b, g - 1)
                threshold(b, G2 - 1)
                f7_lo(b, 0)
                for g in range(G1):
                    if g + 1 < G1:
                        f7_lo(b, g + 1)
                    elif not last:
                        f2_lo(b + 1, 0)
                    residual(b, slot, g)

            images(dve, image)


def _hadamard(n):
    import numpy as _np

    h = _np.ones((1, 1), _np.float32)
    while h.shape[0] < n:
        h = _np.block([[h, h], [h, -h]])
    return h


def kernel(x, L0_conv_v, L0_conv_W, L0_conv_T):
    import numpy as _np
    import concourse.bacc as _bacc
    from concourse import mybir as _mybir
    from concourse.bass_utils import run_bass_kernel_spmd as _run

    nc = _bacc.Bacc("TRN2", target_bir_lowering=False, num_devices=1)
    h_outer = _np.zeros((128, 128), _np.float32)
    for q in range(4):
        h_outer[32 * q:32 * q + 32, 32 * q:32 * q + 32] = _hadamard(32)
    given = {
        "x": x, "v": L0_conv_v, "W": L0_conv_W, "T": L0_conv_T,
        "h_outer": h_outer, "h_inner": _hadamard(128), "eye": _np.eye(128, dtype=_np.float32),
    }
    arrays, args = {}, []
    for name, a in given.items():
        a = _np.ascontiguousarray(a)
        arrays[f"in_{name}_dram"] = a
        args.append(nc.dram_tensor(f"in_{name}_dram", a.shape, _mybir.dt.from_np(a.dtype), kind="ExternalInput").ap())
    args.append(nc.dram_tensor("out_dram", x.shape, _mybir.dt.float32, kind="ExternalOutput").ap())
    spectral_conv_kernel(nc, *args)
    r = _run(nc, [arrays], core_ids=[0])
    return r.results[0]["out_dram"]
```

```python
import concourse.bass as bass
from concourse import mybir
from contextlib import ExitStack


def spectral_conv_kernel(nc, x, v, W, T, h_outer, h_inner, eye, out):
    f32 = mybir.dt.float32
    f32r = mybir.dt.float32r
    f16 = mybir.dt.float16
    ALU = mybir.AluOpType
    ACT = mybir.ActivationFunctionType

    B, C, HH, WW = x.shape
    P = W.shape[0]
    L = 128
    N = HH * WW
    R = N // L
    CA = L // R
    CB = C // CA
    HALF = C // L
    BANK = 512
    TPB = BANK // L
    G1 = CB // TPB
    RPG = BANK // (HALF * L)
    G2 = R // RPG
    NCH = 8
    GPC = G1 // NCH
    PO = P * C
    FR = 4
    LEAD = 8
    F6_AT = 4
    AHEAD = 2
    F6R = 4
    WHOLE = [8,14]
    STEP1_AT = [-2,-1,0,2,4,6,8,10] 
    S2_AT = 14
    BY_POOL = []
    DF = 0
    START = "sasf" 
    SCALE = 1.0 / 16
    PAIRS = B // 2
    assert PO == BANK and C == HALF * L and CB % NCH == 0

    x_v = x.rearrange("b (cb ca) (a h) w -> b (ca a) cb (h w)", ca=CA, a=R)
    out_v = out.rearrange("b (cb ca) (a h) w -> b (ca a) cb (h w)", ca=CA, a=R)
    w_v = W.rearrange("p (oh q) c -> q p oh c", q=L)
    v_v = v.rearrange("p (r h) w -> (p r) (h w)", r=R)
    t_v = T.rearrange("p (r h) w -> (p r) (h w)", r=R)

    ctx = ExitStack()
    with ctx:
        def sb(name, shape, dt):
            return ctx.enter_context(nc.sbuf_tensor(name, shape, dt))

        def sem(name):
            return ctx.enter_context(nc.semaphore(name))

        xs = sb("xs", [L, 2, CB, L], f32)
        f1hi = sb("f1hi", [L, R, CB, CA], f16)
        f1lo = sb("f1lo", [L, R, CB, CA], f16)
        f2hi = sb("f2hi", [L, 2, RPG, HALF, L], f32r)
        f2lo = sb("f2lo", [L, 2, RPG, HALF, L], f32r)
        f4 = sb("f4", [L, FR, RPG, C], f32)
        over = sb("over", [L, FR, RPG, C], f32)
        under = sb("under", [L, FR, RPG, C], f32)
        credit = sb("credit", [L, 2], f32)
        f6 = sb("f6", [L, C, R], f32)
        f6hi = sb("f6hi", [L, F6R, BANK], f16)
        f6lo = sb("f6lo", [L, F6R, BANK], f16)
        f7hi = sb("f7hi", [L, F6R, BANK], f32r)
        f7lo = sb("f7lo", [L, F6R, BANK], f32r)
        f7 = sb("f7", [L, 2, BANK], f32)
        ysc = sb("ysc", [L, 2, BANK], f32)
        w_nat = f6[:, 0:P * HALF * C // R, :].rearrange("q a r -> q (a r)").rearrange(
            "q (p oh c) -> q p oh c", p=P, oh=HALF)
        wThi = sb("wThi", [L, HALF, PO], f32r)
        wTlo = sb("wTlo", [L, HALF, PO], f32r)
        vt_nat = sb("vt_nat", [L, L], f32)
        vt = sb("vt", [L, 2, P, R], f32)
        neg_vt = sb("neg_vt", [L, 2, P, R], f32)
        h32 = sb("h32", [L, L], f32)
        h32r = sb("h32r", [L, L], f32r)
        h128 = sb("h128", [L, L], f32)
        h128h = sb("h128h", [L, L], f16)
        ident = sb("ident", [L, L], f32)
        ps = ctx.enter_context(nc.psum_tensor("ps", [L, 8, BANK], f32))
        S1 = [(2, 3, 0, 1, 6, 7, 5, 4)[g] if g < 8 else g % 2 for g in range(G1)]
        S1_BEFORE = {g: max(e for e in range(g) if S1[e] == S1[g]) for g in range(G1) if S1[g] in S1[:g]}
        S2 = 0
        S3 = (6, 7, 5, 4)
        S4 = [(6, 7, 2)[g % 3] for g in range(G1)]
        S5 = [(4, 5, 3)[g % 3] for g in range(G1)]
        WT_BANK = 4

        consts_in = sem("consts_in")
        w_in = sem("w_in")
        vt_in = sem("vt_in")
        x_in = [sem(f"x_in{k}") for k in range(NCH)]
        y_out = [sem(f"y_out{k}") for k in range(NCH)]
        w_turned = sem("w_turned")
        vt_turned = sem("vt_turned")
        wT_hi = sem("wT_hi")
        wT_ready = sem("wT_ready")
        vt_ready = sem("vt_ready")
        neg_ready = sem("neg_ready")
        hr_ready = sem("hr_ready")
        step1_done = sem("step1_done")
        f1hi_ready = sem("f1hi_ready")
        f1lo_ready = sem("f1lo_ready")
        step2_done = sem("step2_done")
        f2hi_ready = sem("f2hi_ready")
        f2lo_ready = sem("f2lo_ready")
        step3_done = sem("step3_done")
        f4_ready = sem("f4_ready")
        sum_high_ready = sem("sum_high_ready")
        sum_low_ready = sem("sum_low_ready")
        f6_ready = sem("f6_ready")
        f6hi_ready = sem("f6hi_ready")
        f6lo_ready = sem("f6lo_ready")
        step4_done = sem("step4_done")
        f7hi_ready = sem("f7hi_ready")
        f7lo_ready = sem("f7lo_ready")
        step5_done = sem("step5_done")
        y_ready = sem("y_ready")
        y_scaled = sem("y_scaled")
        y_pool_ready = sem("y_pool_ready")
        f6lo_first = sem("f6lo_first")
        S4_FIRST = {g: S1.index(S4[g]) for g in range(3)}
        S5_FIRST = {g: S1.index(S5[g]) for g in range(3)}
        S1_AFTER3 = {S1.index(bank): R - 4 + S3.index(bank) for bank in S3}
        SPLIT = G1 - len(WHOLE)
        SPLIT_TO = [sum(e not in WHOLE for e in range(g + 1)) for g in range(G1)]
        BY_DVE = [g for g in range(G1) if g not in BY_POOL]
        DVE_TO = [sum(e in BY_DVE for e in range(g + 1)) for g in range(G1)]
        POOL_TO = [sum(e in BY_POOL for e in range(g + 1)) for g in range(G1)]
        F6_0 = FR
        Y_0 = 2

        block = ctx.enter_context(nc.Block())

        def images(eng, image):
            with eng.Fori(0, PAIRS - 1) as it:
                for s in range(2):
                    image(it * 2 + s, s, False, False)
            for s in range(2):
                image(B - 2 + s, s, True, s == 1)

        @block.sync
        def _(sp):
            sp.dma_start(h32[:], h_outer).then_inc(consts_in, 16)
            for k in range(NCH):
                q = slice(k * CB // NCH, (k + 1) * CB // NCH)
                sp.dma_start(xs[:, 0, q, :], x_v[0, :, q, :]).then_inc(x_in[k], 16)
            sp.dma_start(ident[:], eye).then_inc(consts_in, 16)
            sp.dma_start(h128[:], h_inner).then_inc(consts_in, 16)
            sp.dma_start(vt_nat[0:P * R, :], v_v).then_inc(vt_in, 16)
            sp.dma_start(vt_nat[P * R:2 * P * R, :], t_v).then_inc(vt_in, 16)
            for p in range(P):
                sp.dma_start(w_nat[:, p, :, :], w_v[:, p, :, :]).then_inc(w_in, 16)
            for k in range(NCH):
                q = slice(k * CB // NCH, (k + 1) * CB // NCH)
                sp.wait_ge(x_in[k], 16)
                sp.dma_start(xs[:, 1, q, :], x_v[1, :, q, :]).then_inc(x_in[k], 16)

            def image(b, slot, last_pair, last):
                for k in range(NCH):
                    q = slice(k * CB // NCH, (k + 1) * CB // NCH)
                    e = GPC * (k + 1) - 1
                    sp.wait_ge(y_ready, Y_0 + len(BY_DVE) * b + DVE_TO[e])
                    if POOL_TO[e]:
                        sp.wait_ge(y_pool_ready, len(BY_POOL) * b + POOL_TO[e])
                    if last_pair:
                        sp.dma_start(out_v[b, :, q, :], xs[:, slot, q, :]).then_inc(y_out[k], 16)
                    else:
                        sp.dma_start(out_v[bass.ds(b, 1), :, q, :].rearrange("b p c j -> p (b c) j"),
                                     xs[:, slot, q, :]).then_inc(y_out[k], 16)
                if not last_pair:
                    for k in range(NCH):
                        q = slice(k * CB // NCH, (k + 1) * CB // NCH)
                        sp.wait_ge(y_out[k], 16 * (b + 1))
                        sp.dma_start(xs[:, slot, q, :],
                                     x_v[bass.ds(b + 2, 1), :, q, :].rearrange("b p c j -> p (b c) j")
                                     ).then_inc(x_in[k], 16)

            images(sp, image)
            for k in range(NCH):
                sp.wait_ge(y_out[k], 16 * B)

        @block.tensor
        def _(pe):
            def step1(b, slot, g, first=False):
                if g % GPC == 0:
                    pe.wait_ge(x_in[g // GPC], 16 * (b + 1))
                if g in S1_AFTER3 and not first:
                    pe.wait_ge(f4_ready, R * (b - 1) + S1_AFTER3[g] + 1)
                if g in S1_BEFORE:
                    pe.wait_ge(f1lo_ready, G1 * b + S1_BEFORE[g] + 1)
                for t in range(TPB):
                    mm = nc.tensor.matmul(ps[:, S1[g], t * L:(t + 1) * L], xs[:, slot, g * TPB + t, :],
                                          h32[:], start=True, stop=True)
                mm.then_inc(step1_done, 1)

            def step2(b, g):
                if g == 0:
                    pe.wait_ge(f1lo_ready, G1 * (b + 1))
                for t in range(TPB):
                    r, half = g * RPG + t // HALF, t % HALF
                    for part in (f1hi, f1lo):
                        mm = nc.tensor.matmul(
                            ps[:, S2 + g % 2, t * L:(t + 1) * L],
                            part[:, r, half * CB // 2:(half + 1) * CB // 2, :].rearrange("p b a -> p (b a)"),
                            h128h[:], start=(part is f1hi), stop=(part is f1lo))
                mm.then_inc(step2_done, 1)

            def step3(b, g):
                s = g % 2
                for k in range(RPG):
                    r = g * RPG + k
                    bank = ps[:, S3[r % 4], :]
                    if r in (2, 3):
                        pe.wait_ge(y_ready, Y_0 + len(BY_DVE) * b + DVE_TO[max(e for e in range(G1) if S5[e] == S3[r])] - len(BY_DVE))
                    elif r >= 4:
                        pe.wait_ge(f4_ready, R * b + r - 3)
                    if k == 0:
                        pe.wait_ge(f2hi_ready, G2 * b + g + 1)
                    for half in range(HALF):
                        nc.tensor.matmul(bank, f2hi[:, s, k, half, :], wTlo[:, half, :], start=(half == 0), stop=False)
                        nc.tensor.matmul(bank, f2hi[:, s, k, half, :], wThi[:, half, :], start=False, stop=False)
                    if k == 0:
                        pe.wait_ge(f2lo_ready, G2 * b + g + 1)
                    for half in range(HALF):
                        mm = nc.tensor.matmul(bank, f2lo[:, s, k, half, :], wThi[:, half, :],
                                              start=False, stop=(half == HALF - 1))
                    mm.then_inc(step3_done, 1)

            def step4(b, g, last):
                if g < DF:
                    pe.wait_ge(f6lo_first, DF * b + g + 1)
                else:
                    pe.wait_ge(f6lo_ready, (G1 - DF) * b + g - DF + 1)
                if g in S4_FIRST and not last:
                    pe.wait_ge(f1lo_ready, G1 * (b + 1) + S4_FIRST[g] + 1)
                for t in range(TPB):
                    for part in (f6hi, f6lo):
                        mm = nc.tensor.matmul(ps[:, S4[g], t * L:(t + 1) * L],
                                              part[:, g % F6R, t * L:(t + 1) * L], h128h[:],
                                              start=(part is f6hi), stop=(part is f6lo))
                mm.then_inc(step4_done, 1)

            def step5(b, g, last):
                bank = ps[:, S5[g], :]
                if g in S5_FIRST and not last:
                    pe.wait_ge(f1lo_ready, G1 * (b + 1) + S5_FIRST[g] + 1)
                if g >= 3:
                    if g - 3 in BY_POOL:
                        pe.wait_ge(y_scaled, len(BY_POOL) * b + POOL_TO[g - 3])
                    else:
                        pe.wait_ge(y_ready, Y_0 + len(BY_DVE) * b + DVE_TO[g - 3])
                pe.wait_ge(f7hi_ready, G1 * b + g + 1)
                if g in WHOLE:
                    nc.tensor.matmul(bank, h32[:], f7[:, WHOLE.index(g) % 2, :],
                                     start=True, stop=True).then_inc(step5_done, 1)
                else:
                    nc.tensor.matmul(bank, h32r[:], f7hi[:, g % F6R, :], start=True, stop=False)
                    pe.wait_ge(f7lo_ready, SPLIT * b + SPLIT_TO[g])
                    nc.tensor.matmul(bank, h32r[:], f7lo[:, g % F6R, :],
                                     start=False, stop=True).then_inc(step5_done, 1)

            pe.wait_ge(consts_in, 48)
            for g in range(G1):
                step1(0, 0, g, first=True)
            pe.wait_ge(w_in, 16 * P)
            pe.wait_ge(f1lo_ready, 8)
            for half in range(HALF):
                for po in range(P * HALF):
                    mm = nc.tensor.transpose(ps[:, WT_BANK + half, po * L:(po + 1) * L],
                                             w_nat[:, po // HALF, po % HALF, half * L:(half + 1) * L], ident[:])
            mm.then_inc(w_turned, 1)
            pe.wait_ge(vt_in, 32)
            nc.tensor.transpose(ps[:, WT_BANK + 2, 0:L], vt_nat[:], ident[:]).then_inc(vt_turned, 1)
            pe.wait_ge(hr_ready, 2)
            step2(0, 0)
            pe.wait_ge(wT_ready, 1)
            pe.wait_ge(vt_ready, 1)

            def image(b, slot, last_pair, last):
                for g in range(G2):
                    if g + 1 < G2:
                        step2(b, g + 1)
                    step3(b, g)
                if not last:
                    for g in range(LEAD):
                        step1(b + 1, 1 - slot, g)
                for g in range(-AHEAD, G1):
                    if g + AHEAD < G1:
                        step4(b, g + AHEAD, last)
                    if g == S2_AT and not last:
                        step2(b + 1, 0)
                    if g >= 0:
                        step5(b, g, last)
                    if g in STEP1_AT and not last:
                        step1(b + 1, 1 - slot, LEAD + STEP1_AT.index(g))

            images(pe, image)

        @block.scalar
        def _(act):
            def f1_hi(b, g):
                act.wait_ge(step1_done, G1 * b + g + 1)
                nc.scalar.copy(f1hi[:, :, g * TPB:(g + 1) * TPB, :].rearrange("j r cb ca -> j (cb ca) r"),
                               ps[:, S1[g], :].rearrange("j (q r) -> j q r", r=R)).then_inc(f1hi_ready, 1)

            def f2_hi(b, g):
                act.wait_ge(step2_done, G2 * b + g + 1)
                if g >= 2:
                    act.wait_ge(step3_done, R * b + RPG * (g - 1))
                nc.scalar.copy(f2hi[:, g % 2, :, :, :].rearrange("c k h i -> c (k h i)"),
                               ps[:, S2 + g % 2, :]).then_inc(f2hi_ready, 1)

            def from_step3(b, g):
                act.wait_ge(f6_ready, F6_0 + G2 * b + g + 1 - FR)
                s = g % FR
                for k in range(RPG):
                    r = g * RPG + k
                    bank = ps[:, S3[r % 4], :]
                    act.wait_ge(step3_done, R * b + r + 1)
                    nc.scalar.activation(f4[:, s, k, :], bank[:, 0:C], ACT.Copy, scale=vt[:, 0, 0, r:r + 1])
                    nc.scalar.activation(over[:, s, k, :], bank[:, C:2 * C], ACT.Relu,
                                         scale=vt[:, 0, 1, r:r + 1], bias=neg_vt[:, 1, 1, r:r + 1])
                    nc.scalar.activation(under[:, s, k, :], bank[:, C:2 * C], ACT.Relu,
                                         scale=neg_vt[:, 0, 1, r:r + 1],
                                         bias=neg_vt[:, 1, 1, r:r + 1]).then_inc(f4_ready, 1)

            def f6_hi(b, g):
                if g >= F6R:
                    act.wait_ge(step4_done, G1 * b + g + 1 - F6R)
                nc.scalar.copy(f6hi[:, g % F6R, :],
                               f6[:, g * TPB * CA:(g + 1) * TPB * CA, :].rearrange("i o r -> i (o r)")
                               ).then_inc(f6hi_ready, 1)

            def f7_hi(b, g):
                act.wait_ge(step4_done, G1 * b + g + 1)
                if g >= F6R:
                    act.wait_ge(step5_done, G1 * b + g + 1 - F6R)
                place = f7[:, WHOLE.index(g) % 2, :] if g in WHOLE else f7hi[:, g % F6R, :]
                nc.scalar.copy(place, ps[:, S4[g], :]).then_inc(f7hi_ready, 1)

            def scale_y(b, g):
                act.wait_ge(step5_done, G1 * b + g + 1)
                n = BY_POOL.index(g)
                act.wait_ge(y_pool_ready, 2 + len(BY_POOL) * b + n + 1 - 2)
                nc.scalar.mul(ysc[:, n % 2, :], ps[:, S5[g], :], 1.0 / (N * SCALE)).then_inc(y_scaled, 1)

            act.wait_ge(consts_in, 48)
            nc.scalar.copy(h32r[:], h32[:]).then_inc(hr_ready, 1)
            nc.scalar.copy(h128h[:], h128[:]).then_inc(hr_ready, 1)
            for g in range(G1):
                f1_hi(0, g)
            act.wait_ge(w_turned, 1)
            nc.scalar.copy(wThi[:], ps[:, WT_BANK:WT_BANK + HALF, :]).then_inc(wT_hi, 1)
            act.wait_ge(vt_turned, 1)
            nc.scalar.activation(vt[:].rearrange("i t p r -> i (t p r)"), ps[:, WT_BANK + 2, 0:L], ACT.Copy,
                                 scale=SCALE).then_inc(vt_ready, 1)
            f2_hi(0, 0)
            act.wait_ge(neg_ready, 1)

            def image(b, slot, last_pair, last):
                for g in range(G2):
                    if g + 1 < G2:
                        f2_hi(b, g + 1)
                    from_step3(b, g)
                if not last:
                    for g in range(F6_AT):
                        f1_hi(b + 1, g)
                act.wait_ge(f6_ready, F6_0 + G2 * (b + 1))
                for g in range(F6R):
                    f6_hi(b, g)
                    if F6_AT + g < LEAD and not last:
                        f1_hi(b + 1, F6_AT + g)
                if not last:
                    for g in range(F6_AT + F6R, LEAD):
                        f1_hi(b + 1, g)
                for g in range(1 - AHEAD, G1):
                    if g + AHEAD - 1 < G1:
                        f7_hi(b, g + AHEAD - 1)
                    if g + AHEAD - 1 + F6R < G1:
                        f6_hi(b, g + AHEAD - 1 + F6R)
                    if g - 1 in STEP1_AT and not last:
                        f1_hi(b + 1, LEAD + STEP1_AT.index(g - 1))
                    if g == S2_AT and not last:
                        f2_hi(b + 1, 0)
                    if g in BY_POOL:
                        scale_y(b, g)

            images(act, image)

        @block.gpsimd
        def _(pool):
            def f6_lo(b, g):
                pool.wait_ge(f6hi_ready, G1 * b + g + 1)
                if g < DF:
                    return
                nc.gpsimd.tensor_tensor(f6lo[:, g % F6R, :],
                                        f6[:, g * TPB * CA:(g + 1) * TPB * CA, :].rearrange("i o r -> i (o r)"),
                                        f6hi[:, g % F6R, :], ALU.subtract).then_inc(f6lo_ready, 1)

            def add_x(b, slot, g):
                n = BY_POOL.index(g)
                pool.wait_ge(y_scaled, len(BY_POOL) * b + n + 1)
                place = xs[:, slot, g * TPB:(g + 1) * TPB, :].rearrange("p c j -> p (c j)")
                nc.gpsimd.tensor_tensor(place, ysc[:, n % 2, :], place, ALU.add).then_inc(y_pool_ready, 1)

            if BY_POOL:
                nc.gpsimd.memset(credit[:, 0:1], 0.0).then_inc(y_pool_ready, 2)

            def image(b, slot, last_pair, last):
                for g in range(G1 + F6R + AHEAD - 1):
                    if g < G1:
                        f6_lo(b, g)
                    if g - (F6R + AHEAD - 1) in BY_POOL:
                        add_x(b, slot, g - (F6R + AHEAD - 1))

            images(pool, image)

        @block.vector
        def _(dve):
            def f2_lo(b, g):
                dve.wait_ge(f2hi_ready, G2 * b + g + 1)
                nc.vector.tensor_tensor(f2lo[:, g % 2, :, :, :].rearrange("c k h i -> c (k h i)"), ps[:, S2 + g % 2, :],
                                        f2hi[:, g % 2, :, :, :].rearrange("c k h i -> c (k h i)").bitcast(f32),
                                        ALU.subtract).then_inc(f2lo_ready, 1)

            def add_high(b, g):
                dve.wait_ge(f4_ready, R * b + RPG * (g + 1))
                for k in range(RPG):
                    r = g * RPG + k
                    add = nc.vector.scalar_tensor_tensor(over[:, g % FR, k, :], f4[:, g % FR, k, :], vt[:, 1, 0, r:r + 1],
                                                         over[:, g % FR, k, :], ALU.max, ALU.add)
                add.then_inc(sum_high_ready, 1)

            def add_low(b, g):
                dve.wait_ge(sum_high_ready, G2 * b + g + 1)
                for k in range(RPG):
                    r = g * RPG + k
                    add = nc.vector.scalar_tensor_tensor(over[:, g % FR, k, :], f4[:, g % FR, k, :],
                                                         neg_vt[:, 1, 0, r:r + 1], over[:, g % FR, k, :],
                                                         ALU.min, ALU.add)
                add.then_inc(sum_low_ready, 1)

            def subtract_under(b, g):
                dve.wait_ge(sum_low_ready, G2 * b + g + 1)
                nc.vector.tensor_tensor(f6[:, :, g * RPG:(g + 1) * RPG].rearrange("i o k -> i k o"),
                                        over[:, g % FR, :, :], under[:, g % FR, :, :],
                                        ALU.subtract).then_inc(f6_ready, 1)

            def f1_lo(b, g):
                dve.wait_ge(f1hi_ready, G1 * b + g + 1)
                place = slice(g * TPB, (g + 1) * TPB)
                nc.vector.tensor_tensor(f1lo[:, :, place, :].rearrange("j r cb ca -> j (cb ca) r"),
                                        ps[:, S1[g], :].rearrange("j (q r) -> j q r", r=R),
                                        f1hi[:, :, place, :].rearrange("j r cb ca -> j (cb ca) r"),
                                        ALU.subtract).then_inc(f1lo_ready, 1)

            def f6_lo_first(b, g):
                dve.wait_ge(f6hi_ready, G1 * b + g + 1)
                nc.vector.tensor_tensor(f6lo[:, g % F6R, :],
                                        f6[:, g * TPB * CA:(g + 1) * TPB * CA, :].rearrange("i o r -> i (o r)"),
                                        f6hi[:, g % F6R, :], ALU.subtract).then_inc(f6lo_first, 1)

            def f7_lo(b, g):
                dve.wait_ge(f7hi_ready, G1 * b + g + 1)
                nc.vector.tensor_tensor(f7lo[:, g % F6R, :], ps[:, S4[g], :], f7hi[:, g % F6R, :].bitcast(f32),
                                        ALU.subtract).then_inc(f7lo_ready, 1)

            def residual(b, slot, g):
                dve.wait_ge(step5_done, G1 * b + g + 1)
                place = xs[:, slot, g * TPB:(g + 1) * TPB, :].rearrange("p c j -> p (c j)")
                nc.vector.scalar_tensor_tensor(place, ps[:, S5[g], :], 1.0 / (N * SCALE), place,
                                               ALU.mult, ALU.add).then_inc(y_ready, 1)

            for g in range(G1):
                f1_lo(0, g)
            dve.wait_ge(wT_hi, 1)
            nc.vector.tensor_tensor(wTlo[:], ps[:, WT_BANK:WT_BANK + HALF, :], wThi[:].bitcast(f32),
                                    ALU.subtract).then_inc(wT_ready, 1)
            dve.wait_ge(vt_ready, 1)
            nc.vector.tensor_scalar(neg_vt[:], vt[:], -1.0, None, ALU.mult).then_inc(neg_ready, 1)
            f2_lo(0, 0)
            dve.wait_ge(neg_ready, 1)
            nc.vector.memset(credit[:, 0:1], 0.0).then_inc(f6_ready, F6_0)
            nc.vector.memset(credit[:, 1:2], 0.0).then_inc(y_ready, Y_0)
            dve.wait_ge(y_ready, Y_0)

            def image(b, slot, last_pair, last):
                for g in range(1, G2 + 1):
                    if g >= 2:
                        add_high(b, g - 2)
                    if g < G2:
                        f2_lo(b, g)
                    if g >= 2:
                        add_low(b, g - 2)
                    if g >= 3:
                        subtract_under(b, g - 3)
                add_high(b, G2 - 1)
                n = 0
                rest = [(subtract_under, G2 - 2), (add_low, G2 - 1), (subtract_under, G2 - 1)]
                for ch in START:
                    if ch == "f":
                        if not last:
                            f1_lo(b + 1, n)
                        n += 1
                    elif ch == "d":
                        for g in range(DF):
                            f6_lo_first(b, g)
                    else:
                        step = rest.pop(0)
                        step[0](b, step[1])
                if not last:
                    for n in range(n, LEAD):
                        f1_lo(b + 1, n)
                for g in range(1 - AHEAD, G1):
                    if g + AHEAD - 1 < G1 and g + AHEAD - 1 not in WHOLE:
                        f7_lo(b, g + AHEAD - 1)
                    if g >= 1 and g - 1 not in BY_POOL:
                        residual(b, slot, g - 1)
                    if g - 1 in STEP1_AT and not last:
                        f1_lo(b + 1, LEAD + STEP1_AT.index(g - 1))
                    if g == S2_AT and not last:
                        f2_lo(b + 1, 0)
                residual(b, slot, G1 - 1)

            images(dve, image)


def _hadamard(n):
    import numpy as _np

    h = _np.ones((1, 1), _np.float32)
    while h.shape[0] < n:
        h = _np.block([[h, h], [h, -h]])
    return h


def kernel(x, L0_conv_v, L0_conv_W, L0_conv_T):
    import numpy as _np
    import concourse.bacc as _bacc
    from concourse import mybir as _mybir
    from concourse.bass_utils import run_bass_kernel_spmd as _run

    nc = _bacc.Bacc("TRN2", target_bir_lowering=False, num_devices=1)
    h_outer = _np.zeros((128, 128), _np.float32)
    for q in range(4):
        h_outer[32 * q:32 * q + 32, 32 * q:32 * q + 32] = _hadamard(32)
    given = {
        "x": x, "v": L0_conv_v, "W": L0_conv_W, "T": L0_conv_T,
        "h_outer": h_outer, "h_inner": _hadamard(128), "eye": _np.eye(128, dtype=_np.float32),
    }
    arrays, args = {}, []
    for name, a in given.items():
        a = _np.ascontiguousarray(a)
        arrays[f"in_{name}_dram"] = a
        args.append(nc.dram_tensor(f"in_{name}_dram", a.shape, _mybir.dt.from_np(a.dtype), kind="ExternalInput").ap())
    args.append(nc.dram_tensor("out_dram", x.shape, _mybir.dt.float32, kind="ExternalOutput").ap())
    spectral_conv_kernel(nc, *args)
    r = _run(nc, [arrays], core_ids=[0])
    return r.results[0]["out_dram"]
```

```python
import concourse.bass as bass
from concourse import mybir
from contextlib import ExitStack


def spectral_conv_kernel(nc, x, v, W, T, h_outer, h_inner, eye, out):
    f32 = mybir.dt.float32
    f32r = mybir.dt.float32r
    f16 = mybir.dt.float16
    ALU = mybir.AluOpType
    ACT = mybir.ActivationFunctionType

    B, C, HH, WW = x.shape
    P = W.shape[0]
    L = 128
    N = HH * WW
    R = N // L
    CA = L // R
    CB = C // CA
    HALF = C // L
    BANK = 512
    TPB = BANK // L
    G1 = CB // TPB
    RPG = BANK // (HALF * L)
    G2 = R // RPG
    NCH = 8
    GPC = G1 // NCH
    PO = P * C
    FR = 4
    F6R = 4
    SCALE = 1.0 / 16
    AHEAD = 2
    LEAD = 9
    ROUND_OF = {LEAD + n: g for n, g in enumerate((-2, 0, 2, 4, 6, 8, 10))}
    GROUP_IN = {g: n for n, g in ROUND_OF.items()}
    STEP2_ROUND = G1 - 2
    F6_AT = 5
    WHOLE = (7, 11, 14)
    PAIRS = B // 2
    assert PO == BANK and C == HALF * L and CB % NCH == 0 and B % 2 == 0 and LEAD + len(ROUND_OF) == G1

    x_v = x.rearrange("b (cb ca) (a h) w -> b (ca a) cb (h w)", ca=CA, a=R)
    out_v = out.rearrange("b (cb ca) (a h) w -> b (ca a) cb (h w)", ca=CA, a=R)
    w_v = W.rearrange("p (oh q) c -> q p oh c", q=L)
    v_v = v.rearrange("p (r h) w -> (p r) (h w)", r=R)
    t_v = T.rearrange("p (r h) w -> (p r) (h w)", r=R)

    ctx = ExitStack()
    with ctx:
        def sb(name, shape, dt):
            return ctx.enter_context(nc.sbuf_tensor(name, shape, dt))

        def sem(name):
            return ctx.enter_context(nc.semaphore(name))

        xs = sb("xs", [L, 2, CB, L], f32)
        f1hi = sb("f1hi", [L, R, CB, CA], f16)
        f1lo = sb("f1lo", [L, R, CB, CA], f16)
        f2hi = sb("f2hi", [L, 2, RPG, HALF, L], f32r)
        f2lo = sb("f2lo", [L, 2, RPG, HALF, L], f32r)
        f4 = sb("f4", [L, FR, RPG, C], f32)
        over = sb("over", [L, FR, RPG, C], f32)
        under = sb("under", [L, FR, RPG, C], f32)
        credit = sb("credit", [L, 2], f32)
        f6 = sb("f6", [L, C, R], f32)
        f6hi = sb("f6hi", [L, F6R, BANK], f16)
        f6lo = sb("f6lo", [L, F6R, BANK], f16)
        f7hi = sb("f7hi", [L, F6R, BANK], f32r)
        f7lo = sb("f7lo", [L, F6R, BANK], f32r)
        f7 = sb("f7", [L, 2, BANK], f32)
        w_nat = f6[:, 0:P * HALF * C // R, :].rearrange("q a r -> q (a r)").rearrange(
            "q (p oh c) -> q p oh c", p=P, oh=HALF)
        wThi = sb("wThi", [L, HALF, PO], f32r)
        wTlo = sb("wTlo", [L, HALF, PO], f32r)
        vt_nat = sb("vt_nat", [L, L], f32)
        vt = sb("vt", [L, 2, P, R], f32)
        neg_vt = sb("neg_vt", [L, 2, P, R], f32)
        h32 = sb("h32", [L, L], f32)
        h32r = sb("h32r", [L, L], f32r)
        h128 = sb("h128", [L, L], f32)
        h128h = sb("h128h", [L, L], f16)
        ident = sb("ident", [L, L], f32)
        ps = ctx.enter_context(nc.psum_tensor("ps", [L, 8, BANK], f32))
        S1 = [(2, 3, 0, 1, 6, 7, 5, 4)[g] if g < 8 else g % 2 for g in range(G1)]
        S2 = 0
        S3 = (6, 7, 5, 4)
        S4 = [(6, 7, 2)[g % 3] for g in range(G1)]
        S5 = [(4, 5, 3)[g % 3] for g in range(G1)]
        TURNED = 4
        S1_BEFORE = {g: max(e for e in range(g) if S1[e] == S1[g]) for g in range(G1) if S1[g] in S1[:g]}
        S3_BEFORE_S1 = {S1.index(bank): R - len(S3) + k for k, bank in enumerate(S3)}
        S1_BEFORE_S4 = {g: S1.index(S4[g]) for g in range(3)}
        S1_BEFORE_S5 = {g: S1.index(S5[g]) for g in range(3)}
        S5_BEFORE_S3 = {r: max(g for g in range(G1) if S5[g] == S3[r]) for r in (2, 3)}

        h32_in = sem("h32_in")
        consts_in = sem("consts_in")
        w_in = sem("w_in")
        vt_in = sem("vt_in")
        x_in = [sem(f"x_in{k}") for k in range(NCH)]
        y_out = [sem(f"y_out{k}") for k in range(NCH)]
        w_turned = sem("w_turned")
        vt_turned = sem("vt_turned")
        wT_hi = sem("wT_hi")
        wT_ready = sem("wT_ready")
        vt_ready = sem("vt_ready")
        neg_ready = sem("neg_ready")
        hr_ready = sem("hr_ready")
        step1_done = sem("step1_done")
        f1hi_ready = sem("f1hi_ready")
        f1lo_ready = sem("f1lo_ready")
        step2_done = sem("step2_done")
        f2hi_ready = sem("f2hi_ready")
        f2lo_ready = sem("f2lo_ready")
        step3_done = sem("step3_done")
        f4_ready = sem("f4_ready")
        sum_high_ready = sem("sum_high_ready")
        sum_low_ready = sem("sum_low_ready")
        f6_ready = sem("f6_ready")
        f6hi_ready = sem("f6hi_ready")
        f6lo_ready = sem("f6lo_ready")
        step4_done = sem("step4_done")
        f7hi_ready = sem("f7hi_ready")
        f7lo_ready = sem("f7lo_ready")
        step5_done = sem("step5_done")
        y_ready = sem("y_ready")
        SPLIT = G1 - len(WHOLE)
        SPLIT_TO = [sum(e not in WHOLE for e in range(g + 1)) for g in range(G1)]
        F6_0 = FR
        Y_0 = 3

        block = ctx.enter_context(nc.Block())

        def images(eng, image):
            with eng.Fori(0, PAIRS - 1) as it:
                for s in range(2):
                    image(it * 2 + s, s, False, False)
            for s in range(2):
                image(B - 2 + s, s, True, s == 1)

        @block.sync
        def _(sp):
            sp.dma_start(h32[:], h_outer).then_inc(h32_in, 16)
            for k in range(NCH):
                q = slice(k * CB // NCH, (k + 1) * CB // NCH)
                sp.dma_start(xs[:, 0, q, :], x_v[0, :, q, :]).then_inc(x_in[k], 16)
            sp.dma_start(ident[:], eye).then_inc(consts_in, 16)
            sp.dma_start(h128[:], h_inner).then_inc(consts_in, 16)
            sp.dma_start(vt_nat[0:P * R, :], v_v).then_inc(vt_in, 16)
            sp.dma_start(vt_nat[P * R:2 * P * R, :], t_v).then_inc(vt_in, 16)
            for p in range(P):
                sp.dma_start(w_nat[:, p, :, :], w_v[:, p, :, :]).then_inc(w_in, 16)
            for k in range(NCH):
                q = slice(k * CB // NCH, (k + 1) * CB // NCH)
                sp.wait_ge(x_in[k], 16)
                sp.dma_start(xs[:, 1, q, :], x_v[1, :, q, :]).then_inc(x_in[k], 16)

            def image(b, slot, last_pair, last):
                for k in range(NCH):
                    q = slice(k * CB // NCH, (k + 1) * CB // NCH)
                    sp.wait_ge(y_ready, Y_0 + G1 * b + GPC * (k + 1))
                    if last_pair:
                        sp.dma_start(out_v[b, :, q, :], xs[:, slot, q, :]).then_inc(y_out[k], 16)
                    else:
                        sp.dma_start(out_v[bass.ds(b, 1), :, q, :].rearrange("b p c j -> p (b c) j"),
                                     xs[:, slot, q, :]).then_inc(y_out[k], 16)
                if not last_pair:
                    for k in range(NCH):
                        q = slice(k * CB // NCH, (k + 1) * CB // NCH)
                        sp.wait_ge(y_out[k], 16 * (b + 1))
                        sp.dma_start(xs[:, slot, q, :],
                                     x_v[bass.ds(b + 2, 1), :, q, :].rearrange("b p c j -> p (b c) j")
                                     ).then_inc(x_in[k], 16)

            images(sp, image)
            for k in range(NCH):
                sp.wait_ge(y_out[k], 16 * B)

        @block.tensor
        def _(pe):
            def step1(b, slot, g, first=False):
                if g % GPC == 0:
                    pe.wait_ge(x_in[g // GPC], 16 * (b + 1))
                if g in S3_BEFORE_S1 and not first:
                    pe.wait_ge(f4_ready, R * (b - 1) + S3_BEFORE_S1[g] + 1)
                if g in S1_BEFORE:
                    pe.wait_ge(f1lo_ready, G1 * b + S1_BEFORE[g] + 1)
                for t in range(TPB):
                    mm = nc.tensor.matmul(ps[:, S1[g], t * L:(t + 1) * L], xs[:, slot, g * TPB + t, :],
                                          h32[:], start=True, stop=True)
                mm.then_inc(step1_done, 1)

            def step2(b, g):
                if g == 0:
                    pe.wait_ge(f1lo_ready, G1 * (b + 1))
                for t in range(TPB):
                    r, half = g * RPG + t // HALF, t % HALF
                    for part in (f1hi, f1lo):
                        mm = nc.tensor.matmul(
                            ps[:, S2 + g % 2, t * L:(t + 1) * L],
                            part[:, r, half * CB // 2:(half + 1) * CB // 2, :].rearrange("p b a -> p (b a)"),
                            h128h[:], start=(part is f1hi), stop=(part is f1lo))
                mm.then_inc(step2_done, 1)

            def step3(b, g):
                s = g % 2
                for k in range(RPG):
                    r = g * RPG + k
                    bank = ps[:, S3[r % 4], :]
                    if r in (2, 3):
                        pe.wait_ge(y_ready, Y_0 + G1 * (b - 1) + S5_BEFORE_S3[r] + 1)
                    elif r >= 4:
                        pe.wait_ge(f4_ready, R * b + r - 3)
                    if k == 0:
                        pe.wait_ge(f2hi_ready, G2 * b + g + 1)
                    for half in range(HALF):
                        nc.tensor.matmul(bank, f2hi[:, s, k, half, :], wTlo[:, half, :], start=(half == 0), stop=False)
                        nc.tensor.matmul(bank, f2hi[:, s, k, half, :], wThi[:, half, :], start=False, stop=False)
                    if k == 0:
                        pe.wait_ge(f2lo_ready, G2 * b + g + 1)
                    for half in range(HALF):
                        mm = nc.tensor.matmul(bank, f2lo[:, s, k, half, :], wThi[:, half, :],
                                              start=False, stop=(half == HALF - 1))
                    mm.then_inc(step3_done, 1)

            def step4(b, g, last):
                pe.wait_ge(f6lo_ready, G1 * b + g + 1)
                if g in S1_BEFORE_S4 and not last:
                    pe.wait_ge(f1lo_ready, G1 * (b + 1) + S1_BEFORE_S4[g] + 1)
                for t in range(TPB):
                    for part in (f6hi, f6lo):
                        mm = nc.tensor.matmul(ps[:, S4[g], t * L:(t + 1) * L],
                                              part[:, g % F6R, t * L:(t + 1) * L], h128h[:],
                                              start=(part is f6hi), stop=(part is f6lo))
                mm.then_inc(step4_done, 1)

            def step5(b, g, last):
                bank = ps[:, S5[g], :]
                if g in S1_BEFORE_S5 and not last:
                    pe.wait_ge(f1lo_ready, G1 * (b + 1) + S1_BEFORE_S5[g] + 1)
                if g >= 3:
                    pe.wait_ge(y_ready, Y_0 + G1 * b + g - 2)
                pe.wait_ge(f7hi_ready, G1 * b + g + 1)
                if g in WHOLE:
                    nc.tensor.matmul(bank, h32[:], f7[:, WHOLE.index(g) % 2, :],
                                     start=True, stop=True).then_inc(step5_done, 1)
                else:
                    nc.tensor.matmul(bank, h32r[:], f7hi[:, g % F6R, :], start=True, stop=False)
                    pe.wait_ge(f7lo_ready, SPLIT * b + SPLIT_TO[g])
                    nc.tensor.matmul(bank, h32r[:], f7lo[:, g % F6R, :],
                                     start=False, stop=True).then_inc(step5_done, 1)

            pe.wait_ge(h32_in, 16)
            for g in range(G1):
                step1(0, 0, g, first=True)
            pe.wait_ge(consts_in, 32)
            pe.wait_ge(w_in, 16 * P)
            pe.wait_ge(f1lo_ready, len(set(S1)))
            for half in range(HALF):
                for po in range(P * HALF):
                    mm = nc.tensor.transpose(ps[:, TURNED + half, po * L:(po + 1) * L],
                                             w_nat[:, po // HALF, po % HALF, half * L:(half + 1) * L], ident[:])
            mm.then_inc(w_turned, 1)
            pe.wait_ge(vt_in, 32)
            nc.tensor.transpose(ps[:, TURNED + 2, 0:L], vt_nat[:], ident[:]).then_inc(vt_turned, 1)
            pe.wait_ge(hr_ready, 2)
            step2(0, 0)
            pe.wait_ge(wT_ready, 1)
            pe.wait_ge(vt_ready, 1)

            def image(b, slot, last_pair, last):
                for g in range(G2):
                    if g + 1 < G2:
                        step2(b, g + 1)
                    step3(b, g)
                if not last:
                    for g in range(LEAD):
                        step1(b + 1, 1 - slot, g)
                for g in range(-AHEAD, G1):
                    if g + AHEAD < G1:
                        step4(b, g + AHEAD, last)
                    if g == STEP2_ROUND and not last:
                        step2(b + 1, 0)
                    if g >= 0:
                        step5(b, g, last)
                    if g in GROUP_IN and not last:
                        step1(b + 1, 1 - slot, GROUP_IN[g])

            images(pe, image)

        @block.scalar
        def _(act):
            def f1_hi(b, g):
                act.wait_ge(step1_done, G1 * b + g + 1)
                nc.scalar.copy(f1hi[:, :, g * TPB:(g + 1) * TPB, :].rearrange("j r cb ca -> j (cb ca) r"),
                               ps[:, S1[g], :].rearrange("j (q r) -> j q r", r=R)).then_inc(f1hi_ready, 1)

            def f2_hi(b, g):
                act.wait_ge(step2_done, G2 * b + g + 1)
                if g >= 2:
                    act.wait_ge(step3_done, R * b + RPG * (g - 1))
                nc.scalar.copy(f2hi[:, g % 2, :, :, :].rearrange("c k h i -> c (k h i)"),
                               ps[:, S2 + g % 2, :]).then_inc(f2hi_ready, 1)

            def from_step3(b, g):
                act.wait_ge(f6_ready, F6_0 + G2 * b + g + 1 - FR)
                s = g % FR
                for k in range(RPG):
                    r = g * RPG + k
                    bank = ps[:, S3[r % 4], :]
                    act.wait_ge(step3_done, R * b + r + 1)
                    nc.scalar.activation(f4[:, s, k, :], bank[:, 0:C], ACT.Copy, scale=vt[:, 0, 0, r:r + 1])
                    nc.scalar.activation(over[:, s, k, :], bank[:, C:2 * C], ACT.Relu,
                                         scale=vt[:, 0, 1, r:r + 1], bias=neg_vt[:, 1, 1, r:r + 1])
                    nc.scalar.activation(under[:, s, k, :], bank[:, C:2 * C], ACT.Relu,
                                         scale=neg_vt[:, 0, 1, r:r + 1],
                                         bias=neg_vt[:, 1, 1, r:r + 1]).then_inc(f4_ready, 1)

            def f6_hi(b, g):
                if g >= F6R:
                    act.wait_ge(step4_done, G1 * b + g + 1 - F6R)
                nc.scalar.copy(f6hi[:, g % F6R, :],
                               f6[:, g * TPB * CA:(g + 1) * TPB * CA, :].rearrange("i o r -> i (o r)")
                               ).then_inc(f6hi_ready, 1)

            def f7_hi(b, g):
                act.wait_ge(step4_done, G1 * b + g + 1)
                if g >= F6R:
                    act.wait_ge(step5_done, G1 * b + g + 1 - F6R)
                place = f7[:, WHOLE.index(g) % 2, :] if g in WHOLE else f7hi[:, g % F6R, :]
                nc.scalar.copy(place, ps[:, S4[g], :]).then_inc(f7hi_ready, 1)

            act.wait_ge(h32_in, 16)
            nc.scalar.copy(h32r[:], h32[:]).then_inc(hr_ready, 1)
            for g in range(G1):
                f1_hi(0, g)
            act.wait_ge(consts_in, 32)
            nc.scalar.copy(h128h[:], h128[:]).then_inc(hr_ready, 1)
            act.wait_ge(w_turned, 1)
            nc.scalar.copy(wThi[:], ps[:, TURNED:TURNED + HALF, :]).then_inc(wT_hi, 1)
            act.wait_ge(vt_turned, 1)
            nc.scalar.activation(vt[:].rearrange("i t p r -> i (t p r)"), ps[:, TURNED + 2, 0:L], ACT.Copy,
                                 scale=SCALE).then_inc(vt_ready, 1)
            f2_hi(0, 0)
            act.wait_ge(neg_ready, 1)

            def image(b, slot, last_pair, last):
                for g in range(G2):
                    if g + 1 < G2:
                        f2_hi(b, g + 1)
                    from_step3(b, g)
                if not last:
                    for g in range(F6_AT):
                        f1_hi(b + 1, g)
                act.wait_ge(f6_ready, F6_0 + G2 * (b + 1))
                for g in range(F6R):
                    f6_hi(b, g)
                    if F6_AT + g < LEAD and not last:
                        f1_hi(b + 1, F6_AT + g)
                if not last:
                    for g in range(F6_AT + F6R, LEAD):
                        f1_hi(b + 1, g)
                for g in range(1 - AHEAD, G1):
                    if g + AHEAD - 1 < G1:
                        f7_hi(b, g + AHEAD - 1)
                    if g + AHEAD - 1 + F6R < G1:
                        f6_hi(b, g + AHEAD - 1 + F6R)
                    if g - 1 in GROUP_IN and not last:
                        f1_hi(b + 1, GROUP_IN[g - 1])
                    if g == STEP2_ROUND and not last:
                        f2_hi(b + 1, 0)

            images(act, image)

        @block.gpsimd
        def _(pool):
            def image(b, slot, last_pair, last):
                for g in range(G1):
                    pool.wait_ge(f6hi_ready, G1 * b + g + 1)
                    nc.gpsimd.tensor_tensor(f6lo[:, g % F6R, :],
                                            f6[:, g * TPB * CA:(g + 1) * TPB * CA, :].rearrange("i o r -> i (o r)"),
                                            f6hi[:, g % F6R, :], ALU.subtract).then_inc(f6lo_ready, 1)

            images(pool, image)

        @block.vector
        def _(dve):
            def f2_lo(b, g):
                dve.wait_ge(f2hi_ready, G2 * b + g + 1)
                nc.vector.tensor_tensor(f2lo[:, g % 2, :, :, :].rearrange("c k h i -> c (k h i)"), ps[:, S2 + g % 2, :],
                                        f2hi[:, g % 2, :, :, :].rearrange("c k h i -> c (k h i)").bitcast(f32),
                                        ALU.subtract).then_inc(f2lo_ready, 1)

            def add_high(b, g):
                dve.wait_ge(f4_ready, R * b + RPG * (g + 1))
                for k in range(RPG):
                    r = g * RPG + k
                    add = nc.vector.scalar_tensor_tensor(over[:, g % FR, k, :], f4[:, g % FR, k, :], vt[:, 1, 0, r:r + 1],
                                                         over[:, g % FR, k, :], ALU.max, ALU.add)
                add.then_inc(sum_high_ready, 1)

            def add_low(b, g):
                dve.wait_ge(sum_high_ready, G2 * b + g + 1)
                for k in range(RPG):
                    r = g * RPG + k
                    add = nc.vector.scalar_tensor_tensor(over[:, g % FR, k, :], f4[:, g % FR, k, :],
                                                         neg_vt[:, 1, 0, r:r + 1], over[:, g % FR, k, :],
                                                         ALU.min, ALU.add)
                add.then_inc(sum_low_ready, 1)

            def subtract_under(b, g):
                dve.wait_ge(sum_low_ready, G2 * b + g + 1)
                nc.vector.tensor_tensor(f6[:, :, g * RPG:(g + 1) * RPG].rearrange("i o k -> i k o"),
                                        over[:, g % FR, :, :], under[:, g % FR, :, :],
                                        ALU.subtract).then_inc(f6_ready, 1)

            def f1_lo(b, g):
                dve.wait_ge(f1hi_ready, G1 * b + g + 1)
                place = slice(g * TPB, (g + 1) * TPB)
                nc.vector.tensor_tensor(f1lo[:, :, place, :].rearrange("j r cb ca -> j (cb ca) r"),
                                        ps[:, S1[g], :].rearrange("j (q r) -> j q r", r=R),
                                        f1hi[:, :, place, :].rearrange("j r cb ca -> j (cb ca) r"),
                                        ALU.subtract).then_inc(f1lo_ready, 1)

            def f7_lo(b, g):
                dve.wait_ge(f7hi_ready, G1 * b + g + 1)
                nc.vector.tensor_tensor(f7lo[:, g % F6R, :], ps[:, S4[g], :], f7hi[:, g % F6R, :].bitcast(f32),
                                        ALU.subtract).then_inc(f7lo_ready, 1)

            def residual(b, slot, g):
                dve.wait_ge(step5_done, G1 * b + g + 1)
                place = xs[:, slot, g * TPB:(g + 1) * TPB, :].rearrange("p c j -> p (c j)")
                nc.vector.scalar_tensor_tensor(place, ps[:, S5[g], :], 1.0 / (N * SCALE), place,
                                               ALU.mult, ALU.add).then_inc(y_ready, 1)

            for g in range(G1):
                f1_lo(0, g)
            dve.wait_ge(wT_hi, 1)
            nc.vector.tensor_tensor(wTlo[:], ps[:, TURNED:TURNED + HALF, :], wThi[:].bitcast(f32),
                                    ALU.subtract).then_inc(wT_ready, 1)
            dve.wait_ge(vt_ready, 1)
            nc.vector.tensor_scalar(neg_vt[:], vt[:], -1.0, None, ALU.mult).then_inc(neg_ready, 1)
            f2_lo(0, 0)
            dve.wait_ge(neg_ready, 1)
            nc.vector.memset(credit[:, 0:1], 0.0).then_inc(f6_ready, F6_0)
            nc.vector.memset(credit[:, 1:2], 0.0).then_inc(y_ready, Y_0)
            dve.wait_ge(y_ready, Y_0)

            def image(b, slot, last_pair, last):
                for g in range(1, G2 + 1):
                    if g >= 2:
                        add_high(b, g - 2)
                    if g < G2:
                        f2_lo(b, g)
                    if g >= 2:
                        add_low(b, g - 2)
                    if g >= 3:
                        subtract_under(b, g - 3)
                add_high(b, G2 - 1)
                subtract_under(b, G2 - 2)
                add_low(b, G2 - 1)
                subtract_under(b, G2 - 1)
                if not last:
                    for g in range(LEAD):
                        f1_lo(b + 1, g)
                for g in range(1 - AHEAD, G1):
                    if g + AHEAD - 1 < G1 and g + AHEAD - 1 not in WHOLE:
                        f7_lo(b, g + AHEAD - 1)
                    if g >= 1:
                        residual(b, slot, g - 1)
                    if g - 1 in GROUP_IN and not last:
                        f1_lo(b + 1, GROUP_IN[g - 1])
                    if g == STEP2_ROUND and not last:
                        f2_lo(b + 1, 0)
                residual(b, slot, G1 - 1)

            images(dve, image)


def _hadamard(n):
    import numpy as _np

    h = _np.ones((1, 1), _np.float32)
    while h.shape[0] < n:
        h = _np.block([[h, h], [h, -h]])
    return h


def kernel(x, L0_conv_v, L0_conv_W, L0_conv_T):
    import numpy as _np
    import concourse.bacc as _bacc
    from concourse import mybir as _mybir
    from concourse.bass_utils import run_bass_kernel_spmd as _run

    nc = _bacc.Bacc("TRN2", target_bir_lowering=False, num_devices=1)
    h_outer = _np.zeros((128, 128), _np.float32)
    for q in range(4):
        h_outer[32 * q:32 * q + 32, 32 * q:32 * q + 32] = _hadamard(32)
    given = {
        "x": x, "v": L0_conv_v, "W": L0_conv_W, "T": L0_conv_T,
        "h_outer": h_outer, "h_inner": _hadamard(128), "eye": _np.eye(128, dtype=_np.float32),
    }
    arrays, args = {}, []
    for name, a in given.items():
        a = _np.ascontiguousarray(a)
        arrays[f"in_{name}_dram"] = a
        args.append(nc.dram_tensor(f"in_{name}_dram", a.shape, _mybir.dt.from_np(a.dtype), kind="ExternalInput").ap())
    args.append(nc.dram_tensor("out_dram", x.shape, _mybir.dt.float32, kind="ExternalOutput").ap())
    spectral_conv_kernel(nc, *args)
    r = _run(nc, [arrays], core_ids=[0])
    return r.results[0]["out_dram"]
```
